# Optimizing a Trainium2 kernel written in Bass

```python
import numpy as np
import jax
import jax.numpy as jnp

def _softmax(x, axis=-1):
    return jax.nn.softmax(x, axis=axis)

def _gelu(x):
    return jax.nn.gelu(x, approximate=True)

def _silu(x):
    return jax.nn.silu(x)

def _sigmoid(x):
    return jax.nn.sigmoid(x)

def _layernorm(x, axis=-1, eps=1e-05):
    m = jnp.mean(x, axis=axis, keepdims=True)
    v = jnp.var(x, axis=axis, keepdims=True)
    return (x - m) / jnp.sqrt(v + eps)

def _scatter_add(tgt, idx, src, axis=0):
    return tgt.at[idx].add(src)

def _segment_sum(src, seg, n):
    return jax.ops.segment_sum(src, seg, n)
kernel_name = 'mk_xattn_seq_d1_seqx_r4_64a807'

def setup_inputs(seed: int=0):
    np.random.seed(seed)
    _w = jnp.asarray

    def _rec_inputs():
        import jax
        import jax.numpy as jnp
        _rk = jax.random.key(seed)
        x = -0.0002928 + 1 * jax.random.normal(jax.random.fold_in(_rk, 1), (8, 512, 256), jnp.float32)
        _lenS = 512 - jax.random.randint(jax.random.fold_in(_rk, 7), (8,), 0, max(1, 512 // 4) + 1, jnp.int32)
        _lenS2 = 512 - jax.random.randint(jax.random.fold_in(_rk, 8), (8,), 0, max(1, 512 // 4) + 1, jnp.int32)
        _ctx_1024P = jax.random.normal(jax.random.fold_in(_rk, 11), (8, 16, 256), jnp.float32)
        _ctx_1024c = jax.random.dirichlet(jax.random.fold_in(_rk, 511), 0.3 * jnp.ones((16,), jnp.float32), (8, 512))
        _ctx_1024t = jnp.einsum('bsk,bkd->bsd', _ctx_1024c, _ctx_1024P)
        _ctx_1024t = _ctx_1024t * jax.lax.rsqrt(jnp.mean(jnp.square(_ctx_1024t)) + 1e-12) * 0.953939
        ctx_1024 = -1.39393e-06 + 0.999914 * (_ctx_1024t + 0.3 * jax.random.normal(jax.random.fold_in(_rk, 611), (8, 512, 256), jnp.float32))
        return (x, ctx_1024)
    x, ctx_1024 = _rec_inputs()

    def _L0_xattn_setup():
        import jax, jax.numpy as jnp
        import numpy as np
        NUM_HEADS = 16
        NEG = float(-2 ** 32 + 1)
        EPS = 1e-08

        def _split_heads(x, H):
            B, S, D = x.shape
            return x.reshape(B, S, H, D // H).transpose(0, 2, 1, 3)
        key = jax.random.key(seed)
        ks = jax.random.split(key, 12)
        B, S, D = (2, 512, 256)
        scale = 1.0 / np.sqrt(D)
        inp = {'queries': jax.random.normal(ks[0], (B, S, D), dtype=jnp.float32), 'keys': jax.random.normal(ks[1], (B, S, D), dtype=jnp.float32), 'values': jax.random.normal(ks[2], (B, S, D), dtype=jnp.float32), 'Wq': jax.random.normal(ks[3], (D, D), dtype=jnp.float32) * scale, 'bq': jnp.zeros((D,), dtype=jnp.float32), 'Wk': jax.random.normal(ks[4], (D, D), dtype=jnp.float32) * scale, 'bk': jnp.zeros((D,), dtype=jnp.float32), 'Wv': jax.random.normal(ks[5], (D, D), dtype=jnp.float32) * scale, 'bv': jnp.zeros((D,), dtype=jnp.float32), 'gamma': jnp.ones((D,), dtype=jnp.float32), 'beta': jnp.zeros((D,), dtype=jnp.float32)}
        return inp
    _L0_xattn_all = _L0_xattn_setup()
    _L0_xattn_in = {k: v for k, v in _L0_xattn_all.items() if k in ('Wq', 'bq', 'Wk', 'bk', 'Wv', 'bv', 'gamma', 'beta')}
    del _L0_xattn_all
    return {'x': x, 'ctx_1024': ctx_1024, 'L0_xattn_Wq': _L0_xattn_in['Wq'], 'L0_xattn_bq': _L0_xattn_in['bq'], 'L0_xattn_Wk': _L0_xattn_in['Wk'], 'L0_xattn_bk': _L0_xattn_in['bk'], 'L0_xattn_Wv': _L0_xattn_in['Wv'], 'L0_xattn_bv': _L0_xattn_in['bv'], 'L0_xattn_gamma': _L0_xattn_in['gamma'], 'L0_xattn_beta': _L0_xattn_in['beta']}

def reference(x, ctx_1024, L0_xattn_Wq, L0_xattn_bq, L0_xattn_Wk, L0_xattn_bk, L0_xattn_Wv, L0_xattn_bv, L0_xattn_gamma, L0_xattn_beta):
    import jax
    import jax.numpy as jnp

    def _L0_xattn_ref(queries, keys, values, Wq, bq, Wk, bk, Wv, bv, gamma, beta):
        import jax, jax.numpy as jnp
        import numpy as np
        NUM_HEADS = 16
        NEG = float(-2 ** 32 + 1)
        EPS = 1e-08

        def _split_heads(x, H):
            B, S, D = x.shape
            return x.reshape(B, S, H, D // H).transpose(0, 2, 1, 3)
        H = NUM_HEADS
        B, S, D = queries.shape
        dh = D // H
        Q = jax.nn.relu(queries @ Wq.T + bq)
        K = jax.nn.relu(keys @ Wk.T + bk)
        V = jax.nn.relu(values @ Wv.T + bv)
        Qh = _split_heads(Q, H)
        Kh = _split_heads(K, H)
        Vh = _split_heads(V, H)
        scores = jnp.einsum('bhqd,bhkd->bhqk', Qh, Kh) / jnp.sqrt(jnp.float32(dh))
        key_mask = jnp.sign(jnp.abs(keys.sum(-1)))
        scores = jnp.where(key_mask[:, None, None, :] == 0.0, NEG, scores)
        causal = jnp.tril(jnp.ones((S, S), dtype=jnp.float32))
        scores = jnp.where(causal[None, None, :, :] == 0.0, NEG, scores)
        attn = jax.nn.softmax(scores, axis=-1)
        query_mask = jnp.sign(jnp.abs(queries.sum(-1)))
        attn = attn * query_mask[:, None, :, None]
        out = jnp.einsum('bhqk,bhkd->bhqd', attn, Vh)
        out = out.transpose(0, 2, 1, 3).reshape(B, S, D)
        out = out + queries
        mean = out.mean(-1, keepdims=True)
        std = jnp.std(out, axis=-1, ddof=1, keepdims=True)
        return gamma * (out - mean) / (std + EPS) + beta
    x = _L0_xattn_ref(x, ctx_1024, ctx_1024, L0_xattn_Wq, L0_xattn_bq, L0_xattn_Wk, L0_xattn_bk, L0_xattn_Wv, L0_xattn_bv, L0_xattn_gamma, L0_xattn_beta)
    return x

_drawn_inputs = setup_inputs


def setup_inputs(seed=0):
    import zlib

    import numpy as np

    out = dict(_drawn_inputs(seed))
    spreads = {'L0_xattn_bq': (0.0, 0.8),
     'L0_xattn_bk': (0.0, 2.0),
     'L0_xattn_bv': (0.0, 0.1),
     'L0_xattn_gamma': (1.0, 0.2),
     'L0_xattn_beta': (0.0, 0.1)}
    factors = {}
    for name, (base, spread) in spreads.items():
        noise = np.random.default_rng([zlib.crc32(name.encode()), seed]).standard_normal(out[name].shape)
        drawn = base * np.exp(spread * noise) if base else spread * noise
        out[name] = jnp.asarray(drawn.astype(out[name].dtype))
    for name, factor in factors.items():
        out[name] = (out[name] * factor).astype(out[name].dtype)
    return out
```

```python
from contextlib import ExitStack

import concourse.bass as bass
from concourse import mybir

F32 = mybir.dt.float32
BF16 = mybir.dt.bfloat16
I32 = mybir.dt.int32
ALU = mybir.AluOpType
ACT = mybir.ActivationFunctionType
AX = mybir.AxisListType

P = 128
B, S, D = 8, 512, 256
H = 16
DH = D // H
NT = S // P
KC = D // P
HALVES = 2
HH = H // HALVES
PAIRS = H // 2
UNITS = 5 * PAIRS
PARTS = 3
Q_ROWS = [0, 1, 2, 0, 1, 0]
K_ROWS = [0, 0, 0, 1, 1, 2]
ROWS = len(Q_ROWS) * DH
VC = 32
NEG = -1.0e30
EPS = 1.0e-8
SQRT_GUESS = float(0x1FBD1DF5)
NEWTON = 3
SCALE = float(DH) ** -0.5

T_LAG = 28
PV_LAG = T_LAG + 2
S_RING, T_RING, P_RING = 2, 2, 4

SIDE = {3: ("M", 1), 4: ("O", 0), 6: ("V", 0), 7: ("V", 1), 9: ("V", 2), 10: ("V", 3), 13: ("O", 1),
        14: ("MASK", 0), 16: ("K", 0), 17: ("Q", 0), 22: ("M", 0), 23: ("O", 2), 24: ("K", 1), 25: ("Q", 1),
        32: ("O", 3), 34: ("VSUM", 0)}
SIDE_BANK = {job: n % 2 for n, job in enumerate(SIDE.values())}
NORM = (37, 38, 39)
DIAG_SLOT = 11
OUT_COPY = {0: 0, 10: 1, 20: 2, 30: 3}
PART_COPIES = {}
for slot, (kind, half) in list(SIDE.items()):
    if kind in ("K", "Q"):
        for part, later in ((0, 3 if kind == "K" else 2), (1, 5 if kind == "K" else 4)):
            PART_COPIES.setdefault(slot + later, []).append((kind, half, part))
OF_PREP = ("V", "MASK", "K", "Q")
JOBS = {k: sum(j[0] == k for j in SIDE.values()) for k in ("M", "O", "V", "VSUM", "MASK", "K", "Q")}
DVE_STEPS, POOL_STEPS = 57, 10
STACK_LOADS = 2 * len(Q_ROWS) * 16


def segments(v, by_key):
    a, b = 2 * (v // 5), 2 * (v // 5) + 1
    pieces = [[(a, 3)], [(b, 3)], [(a, 2), (a, 0)], [(b, 2), (b, 0)], [(a, 1), (b, 1)]][v % 5]
    out, col = [], 0
    for h, q in pieces:
        n = (q + 1) * P
        out.append((h, NT - 1 - q, col, n, col) if by_key else (h, q, col, n, col + n - P))
        col += n
    return out


class Steps:

    def __init__(self, eng, sem):
        self.eng, self.sem, self.base, self.n = eng, sem, 0, 0

    def add(self, ins):
        ins.then_inc(self.sem, 1)
        self.n += 1

    def wait(self):
        self.eng.wait_ge(self.sem, self.base + self.n)

    def done(self, ins):
        self.add(ins)
        self.wait()


def batch_of(job, t):
    if job[0] in OF_PREP:
        return t + 1
    return t - 1 if job[0] == "O" or job == ("M", 1) else t


def nth(job, t):
    kind, i = job
    return batch_of(job, t) * JOBS[kind] + (i + 1)


def present(job, prep, cur, prev):
    if job[0] in OF_PREP:
        return prep
    return prev if job[0] == "O" or job == ("M", 1) else cur


def xattn(nc, xT, ctxT, x, wqT, wkT, wvT, bq, bk, bv, gamma, beta, out):
    with ExitStack() as ctx:
        def sb(name, shape, dt):
            return ctx.enter_context(nc.sbuf_tensor(name, shape, dt))

        def ps(name):
            return ctx.enter_context(nc.psum_tensor(name, [P, 512], F32))

        def sem(name):
            return ctx.enter_context(nc.semaphore(name))

        w_sb = {"K": sb("wk_sb", [P, KC, D], F32), "Q": sb("wq_sb", [P, KC, D], F32)}
        wv_sb = sb("wv_sb", [P, KC, D + 1], F32)
        b_sb = {"K": sb("bk_sb", [P, HALVES], F32), "Q": sb("bq_sb", [P, HALVES], F32)}
        bv_sb = sb("bv_sb", [P, D + 1], F32)
        gamma_sb = sb("gamma_sb", [P, D], F32)
        beta_sb = sb("beta_sb", [P, D], F32)
        ident_f = sb("ident_f", [P, P], F32)
        ident_b = sb("ident_b", [P, P], BF16)
        ones_f = sb("ones_f", [P, P], F32)
        ones_b = sb("ones_b", [P, P], BF16)
        causal_s = sb("causal_s", [P, P], BF16)
        causal_t = sb("causal_t", [P, P], BF16)

        xT_sb = sb("xT_sb", [P, KC, S], F32)
        ctxT_sb = sb("ctxT_sb", [P, KC, S], F32)
        x_sb = [sb(f"x_sb{i}", [P, NT, D], F32) for i in range(2)]
        proj = {"K": sb("proj_k", [P, S], F32), "Q": sb("proj_q", [P, S], F32)}
        rest = {"K": sb("rest_k", [P, S], F32), "Q": sb("rest_q", [P, S], F32)}
        parts = {"K": sb("parts_k", [P, PARTS, S], BF16), "Q": sb("parts_q", [P, PARTS, S], BF16)}
        scratch = {o: nc.dram_tensor(f"scratch_{o}", (D, PARTS, S), BF16, kind="Internal").ap() for o in "KQ"}
        v_raw = [sb(f"v_raw{i}", [P, NT, D + 1], F32) for i in range(2)]
        key_mask = [sb(f"key_mask{i}", [P, NT], F32) for i in range(2)]
        mask_diag = sb("mask_diag", [P, NT, P], BF16)
        mask_row = sb("mask_row", [P, S], F32)
        v_sum_in = sb("v_sum_in", [P, 2, D], F32)
        v_sum = [sb(f"v_sum{i}", [P, D], F32) for i in range(2)]
        v_op = [sb(f"v_op{i}", [P, NT, H, VC], F32) for i in range(2)]
        stack = {o: [sb(f"stack_{o}{i}", [P, H, S], BF16) for i in range(2)] for o in "KQ"}

        block_max = sb("block_max", [P, HALVES, PAIRS // 2, 20], F32)
        row_max = sb("row_max", [P, HH, NT], F32)
        max_rest = sb("max_rest", [P, HH, NT], F32)
        max_parts = [sb(f"max_parts{i}", [P, PARTS, HH * NT], BF16) for i in range(2)]
        max_rows = [sb(f"max_rows{i}", [PARTS * HH * NT, P], BF16) for i in range(2)]

        probs = sb("probs", [P, P_RING, 512], F32)
        oT = [sb(f"oT{i}", [P, S], F32) for i in range(2)]
        query_mask = sb("query_mask", [P, NT], F32)
        x_total = sb("x_total", [P, NT], F32)
        no_key = sb("no_key", [P, 2, NT, 4], F32)
        denom = sb("denom", [P, NT, 4], F32)
        recip = sb("recip", [P, NT, 4], F32)
        factor = sb("factor", [P, NT, 4], F32)
        uniform = sb("uniform", [P, NT, H], F32)
        acc = sb("acc", [P, NT, D], F32)
        tmp = sb("tmp", [P, NT, 64], F32)
        stats = sb("stats", [P, NT, 6], F32)
        mean = sb("mean", [P, NT], F32)
        gap = sb("gap", [P, NT], F32)
        squares = sb("squares", [P, NT], F32)
        half_sq = sb("half_sq", [P, NT], F32)
        half_bits = sb("half_bits", [P, NT], I32)
        root = sb("root", [P, NT], F32)
        quot = sb("quot", [P, NT], F32)
        std_eps = sb("std_eps", [P, NT], F32)
        rstd = sb("rstd", [P, NT], F32)
        y = sb("y", [P, NT, D], F32)

        ps_s = [ps(f"ps_s{i}") for i in range(S_RING)]
        ps_t = [ps(f"ps_t{i}") for i in range(T_RING)]
        ps_o = [ps(f"ps_o{i}") for i in range(2)]
        ps_side = {job: bank for bank_no, bank in enumerate([ps("ps_side0"), ps("ps_side1")])
                   for job, n in SIDE_BANK.items() if n == bank_no}

        w_in = {k: sem(f"w_in_{k}") for k in ("V", "K", "Q", "G")}
        const_ready = sem("const_ready")
        ones_in = sem("ones_in")
        ctx_in = sem("ctx_in")
        xT_in = sem("xT_in")
        x_in = sem("x_in")
        made = {k: sem(f"made_{k}") for k in JOBS}
        read = {k: sem(f"read_{k}") for k in JOBS}
        s_full = sem("s_full")
        s_read = sem("s_read")
        t_full = sem("t_full")
        p_ready = sem("p_ready")
        pv_done = sem("pv_done")
        o_copied = sem("o_copied")
        max_ready = sem("max_ready")
        max_in = [sem(f"max_in{i}") for i in range(2)]
        mask_ready = sem("mask_ready")
        v_ready = sem("v_ready")
        v_sum_ready = sem("v_sum_ready")
        v_op_ready = sem("v_op_ready")
        k_masked = sem("k_masked")
        high_ready = {o: sem(f"high_ready_{o}") for o in "KQ"}
        rest_ready = {o: sem(f"rest_ready_{o}") for o in "KQ"}
        mid_ready = {o: sem(f"mid_ready_{o}") for o in "KQ"}
        low_ready = {o: sem(f"low_ready_{o}") for o in "KQ"}
        scratch_in = [sem(f"scratch_in{i}") for i in range(2)]
        stack_in = [sem(f"stack_in{i}") for i in range(2)]
        uniform_ready = sem("uniform_ready")
        resid_ready = sem("resid_ready")
        y_ready = sem("y_ready")
        y_scaled = sem("y_scaled")
        out_done = sem("out_done")
        dve_steps = sem("dve_steps")
        pool_steps = sem("pool_steps")

 
        N_CONST = 8
        N_W = 2 * 16

        def over_iterations(eng, iteration, steps=None, per=0):
            def count(t0, want):
                if steps:
                    assert steps.n == want, f"{steps.n} steps an iteration, not {want}"

            iteration(-1, 1, True, False, False)
            iteration(0, 0, True, True, False)
            if steps:
                first = steps.n
            with eng.Fori(1, B - 2, 2) as t:
                for k in range(2):
                    if steps:
                        steps.base, steps.n = (t + (k - 1)) * per + first, 0
                    iteration(t + k, (1 + k) % 2, True, True, True)
                    count(t, per)
            if steps:
                steps.base, steps.n = first + (B - 2) * per, 0
            iteration(B - 1, (B - 1) % 2, False, True, True)
            iteration(B, B % 2, False, False, True)


        def since(t, least):
            return t >= least if isinstance(t, int) else True

        def known(eng, value):
            return value if isinstance(value, int) else eng.snap(eng.to_reg(value))

        def of_batch(a, b):
            return a[b] if isinstance(b, int) else a[bass.ds(b, 1)].rearrange("o r c -> (o r) c")

        block = ctx.enter_context(nc.Block())

        @block.sync
        def _(sp):
            def load(key, *pairs):
                for dst, src in pairs:
                    sp.dma_start(dst, src).then_inc(w_in[key], 16)

            def stack_half(t, hf, par):
                loads = known(sp, (t + 1) * STACK_LOADS)
                parts_done = known(sp, (t + 1) * 2 + (hf + 1))
                written = known(sp, (t + 2) * 32)
                banks = known(sp, (t - 1) * UNITS + (hf + 1) * UNITS // 2)
                if since(t, 0):
                    sp.wait_ge(stack_in[hf], loads)
                for o in "KQ":
                    sp.wait_ge(low_ready[o], parts_done)
                    sp.dma_start(scratch[o][hf * P:(hf + 1) * P], parts[o][:]).then_inc(scratch_in[hf], 16)
                sp.wait_ge(scratch_in[hf], written)
                if since(t, 1):
                    sp.wait_ge(t_full, banks)
                for o, rows in (("K", K_ROWS), ("Q", Q_ROWS)):
                    for r, part in enumerate(rows):
                        sp.dma_start(stack[o][1 - par][r * DH:(r + 1) * DH, hf * HH:(hf + 1) * HH, :],
                                     scratch[o][hf * P:(hf + 1) * P, part].rearrange("(h d) t -> d h t", d=DH)
                                     ).then_inc(stack_in[hf], 16)

            def iteration(t, par, prep, cur, prev):
                if prep:
                    read_done = known(sp, nth(("Q", 1), t - 1))
                    srcs = [of_batch(a, t + 1).rearrange("(c p) s -> p c s", p=P) for a in (ctxT, xT)]
                    known(sp, srcs[0].offset * 4)
                    if since(t, 0):
                        sp.wait_ge(made["Q"], read_done)
                    sp.dma_start(ctxT_sb[:], srcs[0]).then_inc(ctx_in, 16)
                    if not since(t, 0):
                        load("V", (wv_sb[:, :, 0:D], wvT.rearrange("(c p) n -> p c n", p=P)),
                             (bv_sb[:, 0:D], bv.partition_broadcast(P)))
                        load("K", (w_sb["K"][:], wkT.rearrange("(c p) n -> p c n", p=P)), (b_sb["K"][:], bk))
                    sp.dma_start(xT_sb[:], srcs[1]).then_inc(xT_in, 16)
                    if not since(t, 0):
                        load("Q", (w_sb["Q"][:], wqT.rearrange("(c p) n -> p c n", p=P)), (b_sb["Q"][:], bq))
                        load("G", (gamma_sb[:], gamma.partition_broadcast(P)), (beta_sb[:], beta.partition_broadcast(P)))
                if prep:
                    stack_half(t, 0, par)
                if cur:
                    src = of_batch(x, t).rearrange("(n p) d -> p n d", p=P)
                    read_done = known(sp, nth(("O", 0), t))
                    known(sp, src.offset * 4)
                    if since(t, 1):
                        sp.wait_ge(resid_ready, read_done)
                    sp.dma_start(x_sb[par][:], src).then_inc(x_in, 16)
                if prep:
                    stack_half(t, 1, par)

            over_iterations(sp, iteration)

        @block.gpsimd
        def _(pool):
            g = nc.gpsimd
            steps = Steps(pool, pool_steps)
            for a in (ident_b, ident_f, causal_s, causal_t):
                steps.add(g.memset(a[:], 0.0))
            steps.wait()
            for a in (ident_b, ident_f):
                g.affine_select(out=a[:], in_=a[:], compare_op=ALU.not_equal, fill=1.0, base=0,
                                pattern=[[-1, P]], channel_multiplier=1).then_inc(const_ready, 1)
            g.affine_select(out=causal_s[:], in_=causal_s[:], compare_op=ALU.is_ge, fill=NEG, base=0,
                            pattern=[[-1, P]], channel_multiplier=1).then_inc(const_ready, 1)
            g.affine_select(out=causal_t[:], in_=causal_t[:], compare_op=ALU.is_ge, fill=NEG, base=0,
                            pattern=[[1, P]], channel_multiplier=-1).then_inc(const_ready, 1)
            for i in range(2):
                steps.add(g.memset(v_op[i][:], 0.0))
            steps.wait()

            def residual(t, i, par):
                prv = 1 - par
                cols = slice(64 * i, 64 * i + 64)
                pool.wait_ge(read["O"], nth(("O", i), t))
                pool.wait_ge(uniform_ready, nth(("O", i), t))
                if i == 0:
                    pool.wait_ge(read["VSUM"], t)
                steps.done(g.tensor_tensor(tmp[:].rearrange("p n (h d) -> p n h d", d=DH),
                                           v_sum[prv][:, cols].rearrange("p (h d) -> p h d", d=DH).unsqueeze(1)
                                           .to_broadcast([P, NT, 4, DH]),
                                           uniform[:, :, 4 * i:4 * i + 4].unsqueeze(3).to_broadcast([P, NT, 4, DH]),
                                           ALU.mult))
                steps.done(g.tensor_tensor(acc[:, :, cols], acc[:, :, cols], tmp[:], ALU.add))
                if i == 0:
                    pool.wait_ge(x_in, t * 16)
                g.tensor_tensor(acc[:, :, cols], acc[:, :, cols], x_sb[prv][:, :, cols], ALU.add)\
                    .then_inc(resid_ready, 1)

            def split(t, hf):
                n = (t + 1) * 2 + hf + 1
                pool.wait_ge(read["MASK"], t + 2)
                pool.wait_ge(read["K"], n)
                g.tensor_tensor(proj["K"][:], proj["K"][:], mask_row[:], ALU.mult).then_inc(k_masked, 1)
                for o in "KQ":
                    pool.wait_ge(high_ready[o], n)
                    g.tensor_tensor(rest[o][:], proj[o][:], parts[o][:, 0, :], ALU.subtract).then_inc(rest_ready[o], 1)
                for o in "KQ":
                    pool.wait_ge(rest_ready[o], n)
                    pool.wait_ge(mid_ready[o], n)
                    g.tensor_tensor(parts[o][:, 2, :], rest[o][:], parts[o][:, 1, :], ALU.subtract)\
                        .then_inc(low_ready[o], 1)

            def iteration(t, par, prep, cur, prev):
                if cur:
                    pool.wait_ge(v_ready, t + 1)
                    if since(t, 1):
                        pool.wait_ge(made["VSUM"], t)
                    steps.done(g.tensor_tensor(v_sum_in[:], v_raw[par][:, 0:2, 0:D], v_raw[par][:, 2:4, 0:D], ALU.add))
                    g.tensor_tensor(v_sum_in[:, 0, :], v_sum_in[:, 0, :], v_sum_in[:, 1, :], ALU.add)\
                        .then_inc(v_sum_ready, 1)
                    if since(t, 1):
                        pool.wait_ge(pv_done, (t - 1) * UNITS + 10)
                    g.tensor_tensor(v_op[par][:, :, :, 0:DH],
                                    v_raw[par][:, :, 0:D].rearrange("p n (h d) -> p n h d", d=DH),
                                    key_mask[par][:].unsqueeze(2).unsqueeze(3).to_broadcast([P, NT, H, DH]),
                                    ALU.mult).then_inc(v_op_ready, 1)
                    g.tensor_copy(v_op[par][:, :, :, DH:DH + 1],
                                  key_mask[par][:].unsqueeze(2).unsqueeze(3).to_broadcast([P, NT, H, 1])
                                  ).then_inc(v_op_ready, 1)
                if prev:
                    residual(t, 0, par)
                    residual(t, 1, par)
                if prep:
                    split(t, 0)
                if prev:
                    residual(t, 2, par)
                if prep:
                    split(t, 1)
                if prev:
                    residual(t, 3, par)
                    pool.wait_ge(y_ready, t * NT)
                    pool.wait_ge(w_in["G"], N_W)
                    steps.done(g.tensor_tensor(y[:], y[:], gamma_sb[:].unsqueeze(1).to_broadcast([P, NT, D]), ALU.mult))
                    g.tensor_tensor(y[:], y[:], beta_sb[:].unsqueeze(1).to_broadcast([P, NT, D]), ALU.add)\
                        .then_inc(y_scaled, 1)
                    pool.wait_ge(y_scaled, t)
                    pool.dma_start(of_batch(out, t - 1).rearrange("(n p) d -> p n d", p=P), y[:]).then_inc(out_done, 16)
                    pool.wait_ge(out_done, t * 16)

            over_iterations(pool, iteration, steps, POOL_STEPS)

        @block.scalar
        def _(act):
            def exponentials(b, v, par):
                n = b * UNITS + v
                act.wait_ge(t_full, n + 1)
                if since(b, 1) or v >= P_RING:
                    act.wait_ge(pv_done, n - P_RING + 1)
                nc.scalar.activation(probs[:, v % P_RING, :], ps_t[v % T_RING][:], ACT.Exp, scale=SCALE)\
                    .then_inc(p_ready, 1)

            def copy_output(t, i):
                n = (t - 1) * 4 + i
                act.wait_ge(pv_done, (t - 1) * UNITS + 10 * (i + 1))
                if i >= 2:
                    act.wait_ge(made["O"], n - 1)
                nc.scalar.activation(oT[i % 2][:], ps_o[i % 2][:], ACT.Copy).then_inc(o_copied, 1)

            def evacuate(t, job, par):
                kind, i = job
                n, bank = nth(job, t), ps_side[job]
                act.wait_ge(made[kind], n)
                if kind == "M":
                    b_par = par if i == 0 else 1 - par
                    nc.scalar.activation(max_rows[i][:], bank[0:PARTS * HH * NT, 0:P // 2].bitcast(BF16),
                                         ACT.Copy).then_inc(read[kind], 1)
                    act.wait_ge(read[kind], n)
                    for r in range(PARTS):
                        act.dma_start(stack["Q"][b_par][ROWS + r:ROWS + r + 1, i * HH:(i + 1) * HH, :]
                                      .rearrange("o h t -> o (h t)"),
                                      max_rows[i][r * HH * NT:(r + 1) * HH * NT, :]).then_inc(max_in[i], 16)
                elif kind == "MASK":
                    if since(t, 0):
                        act.wait_ge(k_masked, 2 * (t + 1))
                    nc.scalar.activation(mask_row[:], bank[:], ACT.Copy).then_inc(read[kind], 1)
                elif kind == "VSUM":
                    if since(t, 1):
                        act.wait_ge(resid_ready, nth(("O", 0), t))
                    nc.scalar.activation(v_sum[par][:], bank[:, 0:D], ACT.Copy).then_inc(read[kind], 1)
                else:
                    if not since(t, 0) and i == 0:
                        act.wait_ge(w_in[kind], N_W)
                    if i or since(t, 0):
                        act.wait_ge(rest_ready[kind], n - 1)
                    nc.scalar.activation(proj[kind][:], bank[:], ACT.Relu, bias=b_sb[kind][:, i:i + 1])\
                        .then_inc(read[kind], 1)

            def part_copies(t, u):
                for o, hf, part in PART_COPIES.get(u, ()):
                    n = (t + 1) * 2 + (hf + 1)
                    if part == 0:
                        act.wait_ge(k_masked if o == "K" else read[o], n)
                        if hf == 1 or since(t, 0):
                            act.wait_ge(scratch_in[1 - hf], (t + (1 + hf)) * 32)
                        nc.scalar.activation(parts[o][:, 0, :], proj[o][:], ACT.Copy).then_inc(high_ready[o], 1)
                    else:
                        act.wait_ge(rest_ready[o], n)
                        nc.scalar.activation(parts[o][:, 1, :], rest[o][:], ACT.Copy).then_inc(mid_ready[o], 1)

            def iteration(t, par, prep, cur, prev):
                for u in range(UNITS):
                    if u >= T_LAG and cur:
                        exponentials(t, u - T_LAG, par)
                    elif u < T_LAG and prev:
                        exponentials(t - 1, u - T_LAG + UNITS, 1 - par)
                    job = SIDE.get(u)
                    if job and job[0] not in "OV" and present(job, prep, cur, prev):
                        evacuate(t, job, par)
                    if u in OUT_COPY and prev:
                        copy_output(t, OUT_COPY[u])
                    if prep:
                        part_copies(t, u)

            act.wait_ge(const_ready, N_CONST)
            for i in range(2):
                act.dma_start(stack["K"][i][ROWS:ROWS + PARTS].rearrange("r h (q t) -> r (h q) t", t=P),
                              ones_b[0:PARTS].unsqueeze(1).to_broadcast([PARTS, H * NT, P])).then_inc(ones_in, 16)
            over_iterations(act, iteration)

        @block.vector
        def _(dve):
            v = nc.vector
            steps = Steps(dve, dve_steps)
            for a, value in ((ones_f[:], 1.0), (ones_b[:], 1.0), (wv_sb[:, :, D:D + 1], 1.0), (bv_sb[:, D:D + 1], 0.0)):
                v.memset(a, value).then_inc(const_ready, 1)
            dve.wait_ge(const_ready, N_CONST)
            dve.wait_ge(w_in["V"], N_W)

            def maxima(t, hf):
                blocks = block_max[:, hf]
                two = blocks[:, :, 8:16].rearrange("p a (h c) -> p a h c", h=2)
                rows = row_max[:].rearrange("p (a h) q -> p a h q", h=2)
                dve.wait_ge(s_read, t * UNITS + (hf + 1) * UNITS // 2)
                steps.add(v.tensor_reduce(rows[:, :, :, 3], blocks[:, :, 0:8].rearrange("p a (h c) -> p a h c", h=2),
                                          AX.X, ALU.max))
                steps.add(v.tensor_reduce(rows[:, :, :, 2], two[:, :, :, 0:3], AX.X, ALU.max))
                steps.add(v.tensor_reduce(rows[:, :, :, 1], blocks[:, :, 16:20].rearrange("p a (h c) -> p a h c", h=2),
                                          AX.X, ALU.max))
                steps.done(v.tensor_copy(rows[:, :, :, 0], two[:, :, :, 3]))
                m = row_max[:].rearrange("p h q -> p (h q)")
                r = max_rest[:].rearrange("p h q -> p (h q)")
                mp = max_parts[hf]
                if since(t, 1):
                    dve.wait_ge(made["M"], 2 * t - 1 + hf)
                steps.done(v.tensor_scalar(mp[:, 0, :], m, -1.0, None, ALU.mult))
                steps.done(v.scalar_tensor_tensor(out=r, in0=m, scalar=-1.0, in1=mp[:, 0, :],
                                                  op0=ALU.mult, op1=ALU.subtract))
                steps.done(v.tensor_copy(mp[:, 1, :], r))
                v.tensor_tensor(mp[:, 2, :], r, mp[:, 1, :], ALU.subtract).then_inc(max_ready, 1)

            def output_group(t, i, par):
                view = ps_side["O", i][:].rearrange("p (q h c) -> p q h c", h=4, c=VC)
                den = view[:, :, :, DH]
                u = uniform[:, :, 4 * i:4 * i + 4]
                missing = no_key[:, i % 2]
                dve.wait_ge(made["O"], nth(("O", i), t))
                steps.done(v.tensor_scalar(missing, den, 0.0, None, ALU.is_equal))
                steps.done(v.scalar_tensor_tensor(out=denom[:], in0=missing, scalar=float(S), in1=den,
                                                  op0=ALU.mult, op1=ALU.add))
                steps.done(v.reciprocal(recip[:], denom[:]))
                steps.done(v.tensor_tensor(factor[:], recip[:], query_mask[:].unsqueeze(2).to_broadcast([P, NT, 4]),
                                           ALU.mult))
                v.tensor_tensor(u, missing, factor[:], ALU.mult).then_inc(uniform_ready, 1)
                v.tensor_tensor(acc[:, :, 64 * i:64 * i + 64].rearrange("p n (h d) -> p n h d", d=DH),
                                view[:, :, :, 0:DH], factor[:].unsqueeze(3).to_broadcast([P, NT, 4, DH]),
                                ALU.mult).then_inc(read["O"], 1)

            def row_stats(t):
                dve.wait_ge(resid_ready, t * 4)
                for q in range(NT):
                    steps.add(v.bn_stats(stats[:, q, :], acc[:, q, :]))

            def row_deviation(t):
                steps.wait()
                mean_e, sq_e, mean_o, sq_o = (stats[:, :, c] for c in (1, 2, 4, 5))
                steps.add(v.tensor_tensor(mean[:], mean_e, mean_o, ALU.add))
                steps.add(v.tensor_tensor(gap[:], mean_e, mean_o, ALU.subtract))
                steps.done(v.tensor_tensor(squares[:], sq_e, sq_o, ALU.add))
                steps.add(v.tensor_scalar(mean[:], mean[:], 0.5, None, ALU.mult))
                steps.done(v.tensor_tensor(gap[:], gap[:], gap[:], ALU.mult))
                steps.done(v.scalar_tensor_tensor(out=squares[:], in0=gap[:], scalar=D / 4.0, in1=squares[:],
                                                  op0=ALU.mult, op1=ALU.add))
                steps.add(v.tensor_scalar(half_bits[:], squares[:].bitcast(I32), 1, None, ALU.logical_shift_right))
                steps.done(v.tensor_scalar(half_sq[:], squares[:], 0.5, None, ALU.mult))
                steps.done(v.tensor_scalar(root[:].bitcast(I32), half_bits[:], SQRT_GUESS, None, ALU.add))
                for _ in range(NEWTON):
                    steps.done(v.reciprocal(quot[:], root[:]))
                    steps.done(v.tensor_tensor(quot[:], half_sq[:], quot[:], ALU.mult))
                    steps.done(v.scalar_tensor_tensor(out=root[:], in0=root[:], scalar=0.5, in1=quot[:],
                                                      op0=ALU.mult, op1=ALU.add))
                steps.done(v.tensor_scalar(std_eps[:], root[:], (D - 1.0) ** -0.5, EPS, ALU.mult, ALU.add))
                steps.add(v.reciprocal(rstd[:], std_eps[:]))

            def row_normalise(t):
                steps.wait()
                for q in range(NT):
                    v.tensor_scalar(y[:, q, :], acc[:, q, :], mean[:, q:q + 1], rstd[:, q:q + 1],
                                    ALU.subtract, ALU.mult).then_inc(y_ready, 1)

            def iteration(t, par, prep, cur, prev):
                for u in range(UNITS):
                    if cur:
                        n = t * UNITS + u
                        dve.wait_ge(s_full, n + 1)
                        v.tensor_reduce(block_max[:, u // 20, u // 5 % 4, u % 5 * 4:u % 5 * 4 + 4],
                                        ps_s[u % S_RING][:].rearrange("p (c k) -> p c k", k=P), AX.X, ALU.max)\
                            .then_inc(s_read, 1)
                    job = SIDE.get(u)
                    if job and present(job, prep, cur, prev):
                        kind, i = job
                        if kind == "O":
                            output_group(t, i, par)
                        elif kind == "V":
                            dve.wait_ge(made["V"], nth(job, t))
                            if i == 0 and since(t, 1):
                                dve.wait_ge(v_op_ready, 2 * t)
                            v.tensor_tensor(v_raw[1 - par][:, i, :], ps_side[job][:, 0:D + 1], bv_sb[:], ALU.add)\
                                .then_inc(read["V"], 1)
                    if u == 2 and prev:
                        dve.wait_ge(x_in, t * 16)
                        steps.done(v.tensor_reduce(x_total[:], x_sb[1 - par][:], AX.X, ALU.add))
                        steps.add(v.tensor_scalar(query_mask[:], x_total[:], 0.0, None, ALU.not_equal))
                    if u == DIAG_SLOT and prep:
                        dve.wait_ge(read["V"], (t + 2) * NT)
                        steps.done(v.tensor_scalar(key_mask[1 - par][:], v_raw[1 - par][:, :, D], 0.0, None, ALU.not_equal))
                        if since(t, 0):
                            dve.wait_ge(made["MASK"], t + 1)
                        for i in range(NT):
                            v.tensor_scalar(mask_diag[:, i, :], ident_b[:], key_mask[1 - par][:, i:i + 1], None,
                                            ALU.mult).then_inc(mask_ready, 1)
                        v.tensor_scalar(v_raw[1 - par][:, :, 0:D], v_raw[1 - par][:, :, 0:D], 0.0, None, ALU.max)\
                            .then_inc(v_ready, 1)
                    if prev and u in NORM:
                        (row_stats, row_deviation, row_normalise)[NORM.index(u)](t)
                    if cur and u in (20, UNITS - 1):
                        maxima(t, u // 21)

            over_iterations(dve, iteration, steps, DVE_STEPS)

        @block.tensor
        def _(pe):
            mm = nc.tensor.matmul
            last_job = [None, None]

            def side(t, job, par):
                kind, i = job
                bank, n = ps_side[job], SIDE_BANK[job]
                if last_job[n]:
                    pe.wait_ge(read[last_job[n][0]], nth(last_job[n], t))
                elif n == 0 and since(t, 0):
                    k_read = nth(("K", 1), t - 1)
                    pe.wait_ge(read["K"], min(k_read, 2 * B) if isinstance(t, int) else k_read)
                elif n == 1 and since(t, 1):
                    pe.wait_ge(read["VSUM"], t)
                elif n == 1 and since(t, 0):
                    pe.wait_ge(read["Q"], nth(("Q", 1), t - 1))
                last_job[n] = job
                if kind in ("V", "K", "Q") and i == 0 and not since(t, 0):
                    pe.wait_ge(w_in[kind], N_W)
                if kind == "V":
                    if i == 0:
                        pe.wait_ge(ctx_in, (t + 2) * 16)
                    for c in range(KC):
                        last = mm(bank[:, 0:D + 1], ctxT_sb[:, c, i * P:(i + 1) * P], wv_sb[:, c, :],
                                  start=(c == 0), stop=(c == KC - 1))
                elif kind == "VSUM":
                    pe.wait_ge(v_sum_ready, t + 1)
                    last = mm(bank[:, 0:D], ones_f[:], v_sum_in[:, 0, :], start=True, stop=True)
                elif kind == "MASK":
                    pe.wait_ge(mask_ready, (t + 2) * NT)
                    last = mm(bank[:], ones_b[:], mask_diag[:].rearrange("p n k -> p (n k)"), start=True, stop=True)
                elif kind in "KQ":
                    if kind == "Q" and i == 0:
                        pe.wait_ge(xT_in, (t + 2) * 16)
                    src = ctxT_sb if kind == "K" else xT_sb
                    for c in range(KC):
                        last = mm(bank[:], w_sb[kind][:, c, i * P:(i + 1) * P], src[:, c, :],
                                  start=(c == 0), stop=(c == KC - 1))
                elif kind == "M":
                    pe.wait_ge(max_ready, nth(job, t))
                    last = nc.tensor.transpose(bank[0:PARTS * HH * NT, 0:P // 2].bitcast(BF16),
                                               max_parts[i][:].rearrange("p r m -> p (r m)"), ident_b[:])
                else:
                    pe.wait_ge(o_copied, nth(job, t))
                    for q in range(NT):
                        last = nc.tensor.transpose(bank[:, q * P:(q + 1) * P], oT[i % 2][:, q * P:(q + 1) * P],
                                                   ident_f[:])
                last.then_inc(made[kind], 1)

            def scores(t, u, par):
                n = t * UNITS + u
                if u % 20 == 0:
                    pe.wait_ge(stack_in[u // 20], (t + 1) * STACK_LOADS)
                if u >= S_RING or since(t, 1):
                    pe.wait_ge(s_read, n - S_RING + 1)
                q_s, k_s, bank = stack["Q"][par], stack["K"][par], ps_s[u % S_RING]
                for h, tile, c, w, d in segments(u, False):
                    mm(bank[:, c:c + w], q_s[0:ROWS, h, tile * P:(tile + 1) * P], k_s[0:ROWS, h, 0:w],
                       start=True, stop=False)
                    last = mm(bank[:, d:d + P], ident_b[:], causal_s[:], start=False, stop=True)
                last.then_inc(s_full, 1)

            def scores_t(b, v, par):
                n = b * UNITS + v
                if v % 20 == 0:
                    pe.wait_ge(max_in[v // 20], (b + 1) * 48)
                    if not since(b, 1):
                        pe.wait_ge(ones_in, 2 * 16)
                if v >= T_RING or since(b, 1):
                    pe.wait_ge(p_ready, n - T_RING + 1)
                q_s, k_s, bank = stack["Q"][par], stack["K"][par], ps_t[v % T_RING]
                for h, tile, c, w, d in segments(v, True):
                    mm(bank[:, c:c + w], k_s[0:ROWS + PARTS, h, tile * P:(tile + 1) * P],
                       q_s[0:ROWS + PARTS, h, S - w:S], start=True, stop=False)
                    last = mm(bank[:, d:d + P], ident_b[:], causal_t[:], start=False, stop=True)
                last.then_inc(t_full, 1)

            def products(b, v, par):
                n = b * UNITS + v
                group = v // 10
                if v == 0:
                    pe.wait_ge(v_op_ready, 2 * (b + 1))
                if v % 10 == 0 and (group >= 2 or group == 0 and since(b, 1)):
                    pe.wait_ge(o_copied, b * 4 + group - 1)
                pe.wait_ge(p_ready, n + 1)
                for h, tile, c, w, _ in segments(v, True):
                    r = h % 4 * VC
                    last = mm(ps_o[group % 2][r:r + VC, S - w:S], v_op[par][:, tile, h, :], probs[:, v % P_RING, c:c + w],
                              start=(tile == 0), stop=(tile == NT - 1), skip_group_check=True)
                last.then_inc(pv_done, 1)

            def iteration(t, par, prep, cur, prev):
                last_job[:] = [None, None]
                for u in range(UNITS):
                    job = SIDE.get(u)
                    if job and present(job, prep, cur, prev):
                        side(t, job, par)
                    if cur:
                        scores(t, u, par)
                    if u >= T_LAG and cur:
                        scores_t(t, u - T_LAG, par)
                    elif u < T_LAG and prev:
                        scores_t(t - 1, u - T_LAG + UNITS, 1 - par)
                    if u >= PV_LAG and cur:
                        products(t, u - PV_LAG, par)
                    elif u < PV_LAG and prev:
                        products(t - 1, u - PV_LAG + UNITS, 1 - par)

            pe.wait_ge(const_ready, N_CONST)
            over_iterations(pe, iteration)


def kernel(**inputs):
    import numpy as np
    import concourse.bacc as bacc
    from concourse.bass_utils import run_bass_kernel_spmd

    nc = bacc.Bacc("TRN2", target_bir_lowering=False, num_devices=1)
    arrays = {
        "xT": np.ascontiguousarray(np.transpose(np.asarray(inputs["x"]), (0, 2, 1))),
        "ctxT": np.ascontiguousarray(np.transpose(np.asarray(inputs["ctx_1024"]), (0, 2, 1))),
        "x": np.ascontiguousarray(inputs["x"]),
        "wqT": np.ascontiguousarray(np.asarray(inputs["L0_xattn_Wq"]).T),
        "wkT": np.ascontiguousarray(np.asarray(inputs["L0_xattn_Wk"]).T),
        "wvT": np.ascontiguousarray(np.asarray(inputs["L0_xattn_Wv"]).T),
        "bq": np.ascontiguousarray(np.asarray(inputs["L0_xattn_bq"]).reshape(HALVES, P).T),
        "bk": np.ascontiguousarray(np.asarray(inputs["L0_xattn_bk"]).reshape(HALVES, P).T),
        "bv": np.ascontiguousarray(inputs["L0_xattn_bv"]),
        "gamma": np.ascontiguousarray(inputs["L0_xattn_gamma"]),
        "beta": np.ascontiguousarray(inputs["L0_xattn_beta"]),
    }
    aps = [nc.dram_tensor(f"in_{n}", a.shape, mybir.dt.from_np(a.dtype), kind="ExternalInput").ap()
           for n, a in arrays.items()]
    out = nc.dram_tensor("out", (B, S, D), F32, kind="ExternalOutput").ap()
    xattn(nc, *aps, out)
    r = run_bass_kernel_spmd(nc, [{f"in_{n}": a for n, a in arrays.items()}], core_ids=[0])
    return r.results[0]["out"]
```

```python
from contextlib import ExitStack

import concourse.bass as bass
from concourse import mybir

F32 = mybir.dt.float32
BF16 = mybir.dt.bfloat16
I32 = mybir.dt.int32
ALU = mybir.AluOpType
ACT = mybir.ActivationFunctionType
AX = mybir.AxisListType

P = 128
B, S, D = 8, 512, 256
H = 16
DH = D // H
NT = S // P
KC = D // P
HALVES = 2
HH = H // HALVES
PAIRS = H // 2
UNITS = 5 * PAIRS
PARTS = 3
Q_ROWS = [0, 1, 2, 0, 1, 0]
K_ROWS = [0, 0, 0, 1, 1, 2]
ROWS = len(Q_ROWS) * DH
VC = 32
NEG = -1.0e30
EPS = 1.0e-8
SQRT_GUESS = float(0x1FBD1DF5)
NEWTON = 3
SCALE = float(DH) ** -0.5

T_LAG = 28
PV_LAG = T_LAG + 2
S_RING, T_RING, P_RING = 2, 2, 4

SIDE = {3: ("M", 1), 5: ("O", 0), 7: ("V", 0), 8: ("V", 1), 10: ("V", 2), 11: ("V", 3), 13: ("O", 1),
        15: ("MASK", 0), 17: ("K", 0), 18: ("Q", 0), 23: ("M", 0), 24: ("O", 2), 25: ("K", 1), 26: ("Q", 1),
        32: ("O", 3), 34: ("VSUM", 0)}
SIDE_BANK = {job: n % 2 for n, job in enumerate(SIDE.values())}
MAXIMA = {20: (0, 0), 21: (0, 1), 39: (1, 0), 0: (1, 1)}
NORM = {35: 0, 36: 1, 37: 2, 38: 3, 1: 4, 2: 5, 3: 6}
LATE = 5
Y_SLOT = 3
DIAG_SLOT = 12
RELU_SLOT = 16
X_SLOT = 17
OUT_COPY = {0: 0, 10: 1, 20: 2, 30: 3}
PART_COPIES = {}
for slot, (kind, half) in list(SIDE.items()):
    if kind in ("K", "Q"):
        for part, later in ((0, 3 if kind == "K" else 2), (1, 5 if kind == "K" else 4)):
            PART_COPIES.setdefault(slot + later, []).append((kind, half, part))
OF_PREP = ("V", "MASK", "K", "Q")
JOBS = {k: sum(j[0] == k for j in SIDE.values()) for k in ("M", "O", "V", "VSUM", "MASK", "K", "Q")}
DVE_STEPS, POOL_STEPS = 57, 10
STACK_LOADS = 2 * len(Q_ROWS) * 16


def segments(v, by_key):
    a, b = 2 * (v // 5), 2 * (v // 5) + 1
    pieces = [[(a, 3)], [(b, 3)], [(a, 2), (a, 0)], [(b, 2), (b, 0)], [(a, 1), (b, 1)]][v % 5]
    out, col = [], 0
    for h, q in pieces:
        n = (q + 1) * P
        out.append((h, NT - 1 - q, col, n, col) if by_key else (h, q, col, n, col + n - P))
        col += n
    return out


class Steps:

    def __init__(self, eng, sem):
        self.eng, self.sem, self.base, self.n = eng, sem, 0, 0

    def add(self, ins):
        ins.then_inc(self.sem, 1)
        self.n += 1

    def wait(self):
        self.eng.wait_ge(self.sem, self.base + self.n)

    def done(self, ins):
        self.add(ins)
        self.wait()


def batch_of(job, t):
    if job[0] in OF_PREP:
        return t + 1
    return t - 1 if job[0] == "O" or job == ("M", 1) else t


def nth(job, t):
    kind, i = job
    return batch_of(job, t) * JOBS[kind] + (i + 1)


def present(job, prep, cur, prev):
    if job[0] in OF_PREP:
        return prep
    return prev if job[0] == "O" or job == ("M", 1) else cur


def xattn(nc, xT, ctxT, x, wqT, wkT, wvT, bq, bk, bv, gamma, beta, out):
    with ExitStack() as ctx:
        def sb(name, shape, dt):
            return ctx.enter_context(nc.sbuf_tensor(name, shape, dt))

        def ps(name):
            return ctx.enter_context(nc.psum_tensor(name, [P, 512], F32))

        def sem(name):
            return ctx.enter_context(nc.semaphore(name))

        w_sb = {"K": sb("wk_sb", [P, KC, D], F32), "Q": sb("wq_sb", [P, KC, D], F32)}
        wv_sb = sb("wv_sb", [P, KC, D + 1], F32)
        b_sb = {"K": sb("bk_sb", [P, HALVES], F32), "Q": sb("bq_sb", [P, HALVES], F32)}
        bv_sb = sb("bv_sb", [P, D + 1], F32)
        gamma_sb = sb("gamma_sb", [P, D], F32)
        beta_sb = sb("beta_sb", [P, D], F32)
        ident_f = sb("ident_f", [P, P], F32)
        ident_b = sb("ident_b", [P, P], BF16)
        ones_f = sb("ones_f", [P, P], F32)
        ones_b = sb("ones_b", [P, P], BF16)
        causal_s = sb("causal_s", [P, P], BF16)
        causal_t = sb("causal_t", [P, P], BF16)

        xT_sb = sb("xT_sb", [P, KC, S], F32)
        ctxT_sb = sb("ctxT_sb", [P, KC, S], F32)
        x_sb = [sb(f"x_sb{i}", [P, NT, D], F32) for i in range(2)]
        proj = {"K": sb("proj_k", [P, S], F32), "Q": sb("proj_q", [P, S], F32)}
        rest = {"K": sb("rest_k", [P, S], F32), "Q": sb("rest_q", [P, S], F32)}
        parts = {"K": sb("parts_k", [P, PARTS, S], BF16), "Q": sb("parts_q", [P, PARTS, S], BF16)}
        scratch = {o: nc.dram_tensor(f"scratch_{o}", (D, PARTS, S), BF16, kind="Internal").ap() for o in "KQ"}
        v_raw = [sb(f"v_raw{i}", [P, NT, D + 1], F32) for i in range(2)]
        key_mask = [sb(f"key_mask{i}", [P, NT], F32) for i in range(2)]
        mask_diag = sb("mask_diag", [P, NT, P], BF16)
        mask_row = sb("mask_row", [P, S], F32)
        v_sum_in = sb("v_sum_in", [P, 2, D], F32)
        v_sum = [sb(f"v_sum{i}", [P, D], F32) for i in range(2)]
        v_op = [sb(f"v_op{i}", [P, NT, H, VC], F32) for i in range(2)]
        stack = {o: [sb(f"stack_{o}{i}", [P, H, S], BF16) for i in range(2)] for o in "KQ"}

        block_max = sb("block_max", [P, HALVES, PAIRS // 2, 20], F32)
        row_max = sb("row_max", [P, HH, NT], F32)
        max_rest = sb("max_rest", [P, HH, NT], F32)
        max_parts = [sb(f"max_parts{i}", [P, PARTS, HH * NT], BF16) for i in range(2)]
        max_rows = [sb(f"max_rows{i}", [PARTS * HH * NT, P], BF16) for i in range(2)]

        probs = sb("probs", [P, P_RING, 512], F32)
        oT = [sb(f"oT{i}", [P, S], F32) for i in range(2)]
        query_mask = [sb(f"query_mask{i}", [P, NT], F32) for i in range(2)]
        x_total = sb("x_total", [P, NT], F32)
        no_key = sb("no_key", [P, 2, NT, 4], F32)
        denom = sb("denom", [P, NT, 4], F32)
        recip = sb("recip", [P, NT, 4], F32)
        factor = sb("factor", [P, NT, 4], F32)
        uniform = sb("uniform", [P, NT, H], F32)
        acc = sb("acc", [P, NT, D], F32)
        tmp = sb("tmp", [P, NT, 64], F32)
        stats = sb("stats", [P, NT, 6], F32)
        mean = sb("mean", [P, NT], F32)
        gap = sb("gap", [P, NT], F32)
        squares = sb("squares", [P, NT], F32)
        half_sq = sb("half_sq", [P, NT], F32)
        half_bits = sb("half_bits", [P, NT], I32)
        root = sb("root", [P, NT], F32)
        shift = sb("shift", [P, NT], F32)
        quot = sb("quot", [P, NT], F32)
        std_eps = sb("std_eps", [P, NT], F32)
        rstd = sb("rstd", [P, NT], F32)
        y = sb("y", [P, NT, D], F32)

        ps_s = [ps(f"ps_s{i}") for i in range(S_RING)]
        ps_t = [ps(f"ps_t{i}") for i in range(T_RING)]
        ps_o = [ps(f"ps_o{i}") for i in range(2)]
        ps_side = {job: bank for bank_no, bank in enumerate([ps("ps_side0"), ps("ps_side1")])
                   for job, n in SIDE_BANK.items() if n == bank_no}

        w_in = {k: sem(f"w_in_{k}") for k in ("V", "K", "Q", "G")}
        const_ready = sem("const_ready")
        ones_in = sem("ones_in")
        ctx_in = sem("ctx_in")
        xT_in = sem("xT_in")
        x_in = sem("x_in")
        made = {k: sem(f"made_{k}") for k in JOBS}
        read = {k: sem(f"read_{k}") for k in JOBS}
        s_full = sem("s_full")
        s_read = sem("s_read")
        t_full = sem("t_full")
        p_ready = sem("p_ready")
        pv_done = sem("pv_done")
        o_copied = sem("o_copied")
        max_ready = sem("max_ready")
        max_in = [sem(f"max_in{i}") for i in range(2)]
        mask_ready = sem("mask_ready")
        v_ready = sem("v_ready")
        v_sum_ready = sem("v_sum_ready")
        v_op_ready = sem("v_op_ready")
        k_masked = sem("k_masked")
        high_ready = {o: sem(f"high_ready_{o}") for o in "KQ"}
        rest_ready = {o: sem(f"rest_ready_{o}") for o in "KQ"}
        mid_ready = {o: sem(f"mid_ready_{o}") for o in "KQ"}
        low_ready = {o: sem(f"low_ready_{o}") for o in "KQ"}
        scratch_in = [sem(f"scratch_in{i}") for i in range(2)]
        stack_in = [sem(f"stack_in{i}") for i in range(2)]
        uniform_ready = sem("uniform_ready")
        norm_ready = sem("norm_ready")
        resid_ready = sem("resid_ready")
        y_ready = sem("y_ready")
        y_scaled = sem("y_scaled")
        out_done = sem("out_done")
        dve_steps = sem("dve_steps")
        pool_steps = sem("pool_steps")

 
        N_CONST = 8
        N_W = 2 * 16

        def over_iterations(eng, iteration, steps=None, per=0):
            def count(t0, want):
                if steps:
                    assert steps.n == want, f"{steps.n} steps an iteration, not {want}"

            iteration(-1, 1, True, False, False)
            iteration(0, 0, True, True, False)
            iteration(1, 1, True, True, True)
            if steps:
                first = steps.n
            with eng.Fori(2, B - 2, 2) as t:
                for k in range(2):
                    if steps:
                        steps.base, steps.n = (t + (k - 2)) * per + first, 0
                    iteration(t + k, k, True, True, True)
                    count(t, per)
            if steps:
                steps.base, steps.n = first + (B - 4) * per, 0
            iteration(B - 2, (B - 2) % 2, True, True, True)
            iteration(B - 1, (B - 1) % 2, False, True, True)
            iteration(B, B % 2, False, False, True)
            iteration(B + 1, (B + 1) % 2, False, False, False)

        def since(t, least):
            return t >= least if isinstance(t, int) else True

        def known(eng, value):
            return value if isinstance(value, int) else eng.snap(eng.to_reg(value))

        def of_batch(a, b):
            return a[b] if isinstance(b, int) else a[bass.ds(b, 1)].rearrange("o r c -> (o r) c")

        def split(eng, isa, t, hf, operands):
            n = (t + 1) * 2 + hf + 1
            if "K" in operands:
                eng.wait_ge(read["MASK"], t + 2)
                eng.wait_ge(read["K"], n)
                isa.tensor_tensor(proj["K"][:], proj["K"][:], mask_row[:], ALU.mult).then_inc(k_masked, 1)
            for o in operands:
                eng.wait_ge(high_ready[o], n)
                isa.tensor_tensor(rest[o][:], proj[o][:], parts[o][:, 0, :], ALU.subtract).then_inc(rest_ready[o], 1)
            for o in operands:
                eng.wait_ge(rest_ready[o], n)
                eng.wait_ge(mid_ready[o], n)
                isa.tensor_tensor(parts[o][:, 2, :], rest[o][:], parts[o][:, 1, :], ALU.subtract)\
                    .then_inc(low_ready[o], 1)

        block = ctx.enter_context(nc.Block())

        @block.sync
        def _(sp):
            def load(key, *pairs):
                for dst, src in pairs:
                    sp.dma_start(dst, src).then_inc(w_in[key], 16)

            def stack_half(t, hf, par):
                loads = known(sp, (t + 1) * STACK_LOADS)
                parts_done = known(sp, (t + 1) * 2 + (hf + 1))
                written = known(sp, (t + 2) * 32)
                banks = known(sp, (t - 1) * UNITS + (hf + 1) * UNITS // 2)
                if since(t, 0):
                    sp.wait_ge(stack_in[hf], loads)
                for o in "KQ":
                    sp.wait_ge(low_ready[o], parts_done)
                    sp.dma_start(scratch[o][hf * P:(hf + 1) * P], parts[o][:]).then_inc(scratch_in[hf], 16)
                sp.wait_ge(scratch_in[hf], written)
                if since(t, 1):
                    sp.wait_ge(t_full, banks)
                for o, rows in (("K", K_ROWS), ("Q", Q_ROWS)):
                    for r, part in enumerate(rows):
                        sp.dma_start(stack[o][1 - par][r * DH:(r + 1) * DH, hf * HH:(hf + 1) * HH, :],
                                     scratch[o][hf * P:(hf + 1) * P, part].rearrange("(h d) t -> d h t", d=DH)
                                     ).then_inc(stack_in[hf], 16)

            def load_batch(b, with_weights=False):
                read_done = known(sp, nth(("Q", 1), b - 2))
                srcs = [of_batch(a, b).rearrange("(c p) s -> p c s", p=P) for a in (ctxT, xT)]
                known(sp, srcs[0].offset * 4)
                if since(b, 1):
                    sp.wait_ge(made["Q"], read_done)
                sp.dma_start(ctxT_sb[:], srcs[0]).then_inc(ctx_in, 16)
                if with_weights:
                    load("V", (wv_sb[:, :, 0:D], wvT.rearrange("(c p) n -> p c n", p=P)),
                         (bv_sb[:, 0:D], bv.partition_broadcast(P)))
                    load("K", (w_sb["K"][:], wkT.rearrange("(c p) n -> p c n", p=P)), (b_sb["K"][:], bk))
                sp.dma_start(xT_sb[:], srcs[1]).then_inc(xT_in, 16)
                if with_weights:
                    load("Q", (w_sb["Q"][:], wqT.rearrange("(c p) n -> p c n", p=P)), (b_sb["Q"][:], bq))

            def iteration(t, par, prep, cur, prev):
                if not since(t, 0):
                    load_batch(0, with_weights=True)
                elif prep and since(t, 1):
                    load_batch(t + 1)
                if cur:
                    src = of_batch(x, t).rearrange("(n p) d -> p n d", p=P)
                    sums = known(sp, t + 1)
                    known(sp, src.offset * 4)
                    if since(t, 1):
                        sp.wait_ge(v_sum_ready, sums)
                    else:
                        load("G", (gamma_sb[:], gamma.partition_broadcast(P)), (beta_sb[:], beta.partition_broadcast(P)))
                    sp.dma_start(x_sb[par][:], src).then_inc(x_in, 16)
                if prep:
                    stack_half(t, 0, par)
                if not since(t, 0):
                    load_batch(1)
                if prep:
                    stack_half(t, 1, par)

            over_iterations(sp, iteration)

        @block.gpsimd
        def _(pool):
            g = nc.gpsimd
            steps = Steps(pool, pool_steps)
            for a in (ident_b, ident_f, causal_s, causal_t):
                steps.add(g.memset(a[:], 0.0))
            steps.wait()
            for a in (ident_b, ident_f):
                g.affine_select(out=a[:], in_=a[:], compare_op=ALU.not_equal, fill=1.0, base=0,
                                pattern=[[-1, P]], channel_multiplier=1).then_inc(const_ready, 1)
            g.affine_select(out=causal_s[:], in_=causal_s[:], compare_op=ALU.is_ge, fill=NEG, base=0,
                            pattern=[[-1, P]], channel_multiplier=1).then_inc(const_ready, 1)
            g.affine_select(out=causal_t[:], in_=causal_t[:], compare_op=ALU.is_ge, fill=NEG, base=0,
                            pattern=[[1, P]], channel_multiplier=-1).then_inc(const_ready, 1)
            for i in range(2):
                steps.add(g.memset(v_op[i][:], 0.0))
            steps.wait()

            def residual(t, i, par):
                prv = 1 - par
                cols = slice(64 * i, 64 * i + 64)
                pool.wait_ge(read["O"], nth(("O", i), t))
                pool.wait_ge(uniform_ready, nth(("O", i), t))
                if i == 0:
                    pool.wait_ge(read["VSUM"], t)
                steps.done(g.tensor_tensor(tmp[:].rearrange("p n (h d) -> p n h d", d=DH),
                                           v_sum[prv][:, cols].rearrange("p (h d) -> p h d", d=DH).unsqueeze(1)
                                           .to_broadcast([P, NT, 4, DH]),
                                           uniform[:, :, 4 * i:4 * i + 4].unsqueeze(3).to_broadcast([P, NT, 4, DH]),
                                           ALU.mult))
                steps.done(g.tensor_tensor(acc[:, :, cols], acc[:, :, cols], tmp[:], ALU.add))
                if i == 0:
                    pool.wait_ge(x_in, t * 16)
                g.tensor_tensor(acc[:, :, cols], acc[:, :, cols], x_sb[prv][:, :, cols], ALU.add)\
                    .then_inc(resid_ready, 1)

            def leave(b):
                pool.wait_ge(y_ready, (b + 1) * NT)
                pool.wait_ge(w_in["G"], N_W)
                steps.done(g.tensor_tensor(y[:], y[:], gamma_sb[:].unsqueeze(1).to_broadcast([P, NT, D]), ALU.mult))
                g.tensor_tensor(y[:], y[:], beta_sb[:].unsqueeze(1).to_broadcast([P, NT, D]), ALU.add)\
                    .then_inc(y_scaled, 1)
                pool.wait_ge(y_scaled, b + 1)
                pool.dma_start(of_batch(out, b).rearrange("(n p) d -> p n d", p=P), y[:]).then_inc(out_done, 16)
                pool.wait_ge(out_done, (b + 1) * 16)

            def iteration(t, par, prep, cur, prev):
                operands = "KQ" if since(t, 0) else "Q"
                if cur:
                    pool.wait_ge(v_ready, t + 1)
                    if since(t, 1):
                        pool.wait_ge(made["VSUM"], t)
                    steps.done(g.tensor_tensor(v_sum_in[:], v_raw[par][:, 0:2, 0:D], v_raw[par][:, 2:4, 0:D], ALU.add))
                    g.tensor_tensor(v_sum_in[:, 0, :], v_sum_in[:, 0, :], v_sum_in[:, 1, :], ALU.add)\
                        .then_inc(v_sum_ready, 1)
                    if since(t, 1):
                        pool.wait_ge(pv_done, (t - 1) * UNITS + 10)
                    g.tensor_tensor(v_op[par][:, :, :, 0:DH],
                                    v_raw[par][:, :, 0:D].rearrange("p n (h d) -> p n h d", d=DH),
                                    key_mask[par][:].unsqueeze(2).unsqueeze(3).to_broadcast([P, NT, H, DH]),
                                    ALU.mult).then_inc(v_op_ready, 1)
                    g.tensor_copy(v_op[par][:, :, :, DH:DH + 1],
                                  key_mask[par][:].unsqueeze(2).unsqueeze(3).to_broadcast([P, NT, H, 1])
                                  ).then_inc(v_op_ready, 1)
                if since(t, 2):
                    leave(t - 2)
                if prev:
                    residual(t, 0, par)
                    residual(t, 1, par)
                if prep:
                    split(pool, g, t, 0, operands)
                if prev:
                    residual(t, 2, par)
                if prep:
                    split(pool, g, t, 1, operands)
                if prev:
                    residual(t, 3, par)

            over_iterations(pool, iteration, steps, POOL_STEPS)

        @block.scalar
        def _(act):
            def exponentials(b, v, par):
                n = b * UNITS + v
                act.wait_ge(t_full, n + 1)
                if since(b, 1) or v >= P_RING:
                    act.wait_ge(pv_done, n - P_RING + 1)
                nc.scalar.activation(probs[:, v % P_RING, :], ps_t[v % T_RING][:], ACT.Exp, scale=SCALE)\
                    .then_inc(p_ready, 1)

            def copy_output(t, i):
                n = (t - 1) * 4 + i
                act.wait_ge(pv_done, (t - 1) * UNITS + 10 * (i + 1))
                if i >= 2:
                    act.wait_ge(made["O"], n - 1)
                nc.scalar.activation(oT[i % 2][:], ps_o[i % 2][:], ACT.Copy).then_inc(o_copied, 1)

            def evacuate(t, job, par):
                kind, i = job
                n, bank = nth(job, t), ps_side[job]
                act.wait_ge(made[kind], n)
                if kind == "M":
                    b_par = par if i == 0 else 1 - par
                    nc.scalar.activation(max_rows[i][:], bank[0:PARTS * HH * NT, 0:P // 2].bitcast(BF16),
                                         ACT.Copy).then_inc(read[kind], 1)
                    act.wait_ge(read[kind], n)
                    for r in range(PARTS):
                        act.dma_start(stack["Q"][b_par][ROWS + r:ROWS + r + 1, i * HH:(i + 1) * HH, :]
                                      .rearrange("o h t -> o (h t)"),
                                      max_rows[i][r * HH * NT:(r + 1) * HH * NT, :]).then_inc(max_in[i], 16)
                elif kind == "MASK":
                    if since(t, 0):
                        act.wait_ge(k_masked, 2 * (t + 1))
                    nc.scalar.activation(mask_row[:], bank[:], ACT.Copy).then_inc(read[kind], 1)
                elif kind == "VSUM":
                    if since(t, 1):
                        act.wait_ge(resid_ready, nth(("O", 0), t))
                    nc.scalar.activation(v_sum[par][:], bank[:, 0:D], ACT.Copy).then_inc(read[kind], 1)
                else:
                    if not since(t, 0) and i == 0:
                        act.wait_ge(w_in[kind], N_W)
                    if i or since(t, 0):
                        act.wait_ge(rest_ready[kind], n - 1)
                    nc.scalar.activation(proj[kind][:], bank[:], ACT.Relu, bias=b_sb[kind][:, i:i + 1])\
                        .then_inc(read[kind], 1)

            def part_copies(t, u):
                for o, hf, part in PART_COPIES.get(u, ()):
                    n = (t + 1) * 2 + (hf + 1)
                    if part == 0:
                        act.wait_ge(k_masked if o == "K" else read[o], n)
                        if hf == 1 or since(t, 0):
                            act.wait_ge(scratch_in[1 - hf], (t + (1 + hf)) * 32)
                        nc.scalar.activation(parts[o][:, 0, :], proj[o][:], ACT.Copy).then_inc(high_ready[o], 1)
                    else:
                        act.wait_ge(rest_ready[o], n)
                        nc.scalar.activation(parts[o][:, 1, :], rest[o][:], ACT.Copy).then_inc(mid_ready[o], 1)

            def iteration(t, par, prep, cur, prev):
                for u in range(UNITS):
                    if u >= T_LAG and cur:
                        exponentials(t, u - T_LAG, par)
                    elif u < T_LAG and prev:
                        exponentials(t - 1, u - T_LAG + UNITS, 1 - par)
                    job = SIDE.get(u)
                    if job and job[0] not in "OV" and present(job, prep, cur, prev):
                        evacuate(t, job, par)
                    if u in OUT_COPY and prev:
                        copy_output(t, OUT_COPY[u])
                    if prep:
                        part_copies(t, u)
                    if since(t, 2) and Y_SLOT <= u < Y_SLOT + 2:
                        act.wait_ge(norm_ready, t - 1)
                        for q in range(2 * (u - Y_SLOT), 2 * (u - Y_SLOT) + 2):
                            nc.scalar.activation(y[:, q, :], acc[:, q, :], ACT.Identity, bias=shift[:, q:q + 1],
                                                 scale=rstd[:, q:q + 1]).then_inc(y_ready, 1)

            act.wait_ge(const_ready, N_CONST)
            for i in range(2):
                act.dma_start(stack["K"][i][ROWS:ROWS + PARTS].rearrange("r h (q t) -> r (h q) t", t=P),
                              ones_b[0:PARTS].unsqueeze(1).to_broadcast([PARTS, H * NT, P])).then_inc(ones_in, 16)
            over_iterations(act, iteration)

        @block.vector
        def _(dve):
            v = nc.vector
            steps = Steps(dve, dve_steps)
            for a, value in ((ones_f[:], 1.0), (ones_b[:], 1.0), (wv_sb[:, :, D:D + 1], 1.0), (bv_sb[:, D:D + 1], 0.0)):
                v.memset(a, value).then_inc(const_ready, 1)
            dve.wait_ge(const_ready, N_CONST)
            dve.wait_ge(w_in["V"], N_W)

            def maxima(b, hf, step):
                m = row_max[:].rearrange("p h q -> p (h q)")
                r = max_rest[:].rearrange("p h q -> p (h q)")
                mp = max_parts[hf]
                if step == 0:
                    blocks = block_max[:, hf]
                    two = blocks[:, :, 8:16].rearrange("p a (h c) -> p a h c", h=2)
                    rows = row_max[:].rearrange("p (a h) q -> p a h q", h=2)
                    dve.wait_ge(s_read, b * UNITS + (hf + 1) * UNITS // 2)
                    steps.add(v.tensor_reduce(rows[:, :, :, 3], blocks[:, :, 0:8].rearrange("p a (h c) -> p a h c", h=2),
                                              AX.X, ALU.max))
                    steps.add(v.tensor_reduce(rows[:, :, :, 2], two[:, :, :, 0:3], AX.X, ALU.max))
                    steps.add(v.tensor_reduce(rows[:, :, :, 1], blocks[:, :, 16:20].rearrange("p a (h c) -> p a h c", h=2),
                                              AX.X, ALU.max))
                    steps.done(v.tensor_copy(rows[:, :, :, 0], two[:, :, :, 3]))
                    if hf == 0 and since(b, 1):
                        dve.wait_ge(made["M"], 2 * b - 1)
                    steps.add(v.tensor_scalar(mp[:, 0, :], m, -1.0, None, ALU.mult))
                else:
                    steps.wait()
                    steps.done(v.scalar_tensor_tensor(out=r, in0=m, scalar=-1.0, in1=mp[:, 0, :],
                                                      op0=ALU.mult, op1=ALU.subtract))
                    steps.done(v.tensor_copy(mp[:, 1, :], r))
                    v.tensor_tensor(mp[:, 2, :], r, mp[:, 1, :], ALU.subtract).then_inc(max_ready, 1)

            def output_group(t, i, par):
                view = ps_side["O", i][:].rearrange("p (q h c) -> p q h c", h=4, c=VC)
                den = view[:, :, :, DH]
                u = uniform[:, :, 4 * i:4 * i + 4]
                missing = no_key[:, i % 2]
                dve.wait_ge(made["O"], nth(("O", i), t))
                if i == 0 and since(t, 2):
                    dve.wait_ge(y_ready, (t - 1) * NT)
                steps.done(v.tensor_scalar(missing, den, 0.0, None, ALU.is_equal))
                steps.done(v.scalar_tensor_tensor(out=denom[:], in0=missing, scalar=float(S), in1=den,
                                                  op0=ALU.mult, op1=ALU.add))
                steps.done(v.reciprocal(recip[:], denom[:]))
                steps.done(v.tensor_tensor(factor[:], recip[:], query_mask[1 - par][:].unsqueeze(2).to_broadcast([P, NT, 4]),
                                           ALU.mult))
                v.tensor_tensor(u, missing, factor[:], ALU.mult).then_inc(uniform_ready, 1)
                v.tensor_tensor(acc[:, :, 64 * i:64 * i + 64].rearrange("p n (h d) -> p n h d", d=DH),
                                view[:, :, :, 0:DH], factor[:].unsqueeze(3).to_broadcast([P, NT, 4, DH]),
                                ALU.mult).then_inc(read["O"], 1)

            def normalise(b, step):
                mean_e, sq_e, mean_o, sq_o = (stats[:, :, c] for c in (1, 2, 4, 5))
                if step == 0:
                    dve.wait_ge(resid_ready, (b + 1) * 4)
                if step <= 1:
                    for q in range(2 * step, 2 * step + 2):
                        steps.add(v.bn_stats(stats[:, q, :], acc[:, q, :]))
                elif step == 2:
                    steps.wait()
                    steps.add(v.tensor_tensor(mean[:], mean_e, mean_o, ALU.add))
                    steps.add(v.tensor_tensor(squares[:], sq_e, sq_o, ALU.add))
                    steps.done(v.tensor_tensor(gap[:], mean_e, mean_o, ALU.subtract))
                    steps.add(v.tensor_scalar(mean[:], mean[:], 0.5, None, ALU.mult))
                    steps.add(v.tensor_tensor(gap[:], gap[:], gap[:], ALU.mult))
                elif step == 3:
                    steps.wait()
                    steps.done(v.scalar_tensor_tensor(out=squares[:], in0=gap[:], scalar=D / 4.0, in1=squares[:],
                                                      op0=ALU.mult, op1=ALU.add))
                    steps.add(v.tensor_scalar(half_sq[:], squares[:], 0.5, None, ALU.mult))
                    steps.done(v.tensor_scalar(half_bits[:], squares[:].bitcast(I32), 1, None, ALU.logical_shift_right))
                    steps.add(v.tensor_scalar(root[:].bitcast(I32), half_bits[:], SQRT_GUESS, None, ALU.add))
                elif step < 4 + NEWTON:
                    steps.wait()
                    steps.done(v.reciprocal(quot[:], root[:]))
                    steps.done(v.tensor_tensor(quot[:], half_sq[:], quot[:], ALU.mult))
                    steps.add(v.scalar_tensor_tensor(out=root[:], in0=root[:], scalar=0.5, in1=quot[:],
                                                     op0=ALU.mult, op1=ALU.add))
                if step == 3 + NEWTON:
                    steps.wait()
                    steps.done(v.tensor_scalar(std_eps[:], root[:], (D - 1.0) ** -0.5, EPS, ALU.mult, ALU.add))
                    steps.done(v.reciprocal(rstd[:], std_eps[:]))
                    v.scalar_tensor_tensor(out=shift[:], in0=mean[:], scalar=-1.0, in1=rstd[:],
                                           op0=ALU.mult, op1=ALU.mult).then_inc(norm_ready, 1)

            def iteration(t, par, prep, cur, prev):
                for u in range(UNITS):
                    if cur:
                        n = t * UNITS + u
                        dve.wait_ge(s_full, n + 1)
                        v.tensor_reduce(block_max[:, u // 20, u // 5 % 4, u % 5 * 4:u % 5 * 4 + 4],
                                        ps_s[u % S_RING][:].rearrange("p (c k) -> p c k", k=P), AX.X, ALU.max)\
                            .then_inc(s_read, 1)
                    if u in MAXIMA and (cur if u else prev):
                        maxima(t if u else t - 1, *MAXIMA[u])
                    job = SIDE.get(u)
                    if job and present(job, prep, cur, prev):
                        kind, i = job
                        if kind == "O":
                            output_group(t, i, par)
                        elif kind == "V":
                            dve.wait_ge(made["V"], nth(job, t))
                            if i == 0 and since(t, 1):
                                dve.wait_ge(v_op_ready, 2 * t)
                            v.tensor_tensor(v_raw[1 - par][:, i, :], ps_side[job][:, 0:D + 1], bv_sb[:], ALU.add)\
                                .then_inc(read["V"], 1)
                    if u == X_SLOT and cur:
                        dve.wait_ge(x_in, (t + 1) * 16)
                        steps.done(v.tensor_reduce(x_total[:], x_sb[par][:], AX.X, ALU.add))
                        steps.add(v.tensor_scalar(query_mask[par][:], x_total[:], 0.0, None, ALU.not_equal))
                    if u == DIAG_SLOT and prep:
                        dve.wait_ge(read["V"], (t + 2) * NT)
                        steps.done(v.tensor_scalar(key_mask[1 - par][:], v_raw[1 - par][:, :, D], 0.0, None, ALU.not_equal))
                        if since(t, 0):
                            dve.wait_ge(made["MASK"], t + 1)
                        for i in range(NT):
                            v.tensor_scalar(mask_diag[:, i, :], ident_b[:], key_mask[1 - par][:, i:i + 1], None,
                                            ALU.mult).then_inc(mask_ready, 1)
                    if u == RELU_SLOT and prep:
                        v.tensor_scalar(v_raw[1 - par][:, :, 0:D], v_raw[1 - par][:, :, 0:D], 0.0, None, ALU.max)\
                            .then_inc(v_ready, 1)
                    if u in NORM and (since(t, 2) if u < LATE else prev):
                        normalise(t - 2 if u < LATE else t - 1, NORM[u])

                if not since(t, 0):
                    for hf in range(HALVES):
                        split(dve, v, t, hf, "K")

            over_iterations(dve, iteration, steps, DVE_STEPS)

        @block.tensor
        def _(pe):
            mm = nc.tensor.matmul
            last_job = [None, None]

            def side(t, job, par):
                kind, i = job
                bank, n = ps_side[job], SIDE_BANK[job]
                if last_job[n]:
                    pe.wait_ge(read[last_job[n][0]], nth(last_job[n], t))
                elif n == 0 and since(t, 0):
                    k_read = nth(("K", 1), t - 1)
                    pe.wait_ge(read["K"], min(k_read, 2 * B) if isinstance(t, int) else k_read)
                elif n == 1 and since(t, 1):
                    pe.wait_ge(read["VSUM"], t)
                elif n == 1 and since(t, 0):
                    pe.wait_ge(read["Q"], nth(("Q", 1), t - 1))
                last_job[n] = job
                if kind in ("V", "K", "Q") and i == 0 and not since(t, 0):
                    pe.wait_ge(w_in[kind], N_W)
                if kind == "V":
                    if i == 0:
                        pe.wait_ge(ctx_in, (t + 2) * 16)
                    for c in range(KC):
                        last = mm(bank[:, 0:D + 1], ctxT_sb[:, c, i * P:(i + 1) * P], wv_sb[:, c, :],
                                  start=(c == 0), stop=(c == KC - 1))
                elif kind == "VSUM":
                    pe.wait_ge(v_sum_ready, t + 1)
                    last = mm(bank[:, 0:D], ones_f[:], v_sum_in[:, 0, :], start=True, stop=True)
                elif kind == "MASK":
                    pe.wait_ge(mask_ready, (t + 2) * NT)
                    last = mm(bank[:], ones_b[:], mask_diag[:].rearrange("p n k -> p (n k)"), start=True, stop=True)
                elif kind in "KQ":
                    if kind == "Q" and i == 0:
                        pe.wait_ge(xT_in, (t + 2) * 16)
                    src = ctxT_sb if kind == "K" else xT_sb
                    for c in range(KC):
                        last = mm(bank[:], w_sb[kind][:, c, i * P:(i + 1) * P], src[:, c, :],
                                  start=(c == 0), stop=(c == KC - 1))
                elif kind == "M":
                    pe.wait_ge(max_ready, nth(job, t))
                    last = nc.tensor.transpose(bank[0:PARTS * HH * NT, 0:P // 2].bitcast(BF16),
                                               max_parts[i][:].rearrange("p r m -> p (r m)"), ident_b[:])
                else:
                    pe.wait_ge(o_copied, nth(job, t))
                    for q in range(NT):
                        last = nc.tensor.transpose(bank[:, q * P:(q + 1) * P], oT[i % 2][:, q * P:(q + 1) * P],
                                                   ident_f[:])
                last.then_inc(made[kind], 1)

            def scores(t, u, par):
                n = t * UNITS + u
                if u % 20 == 0:
                    pe.wait_ge(stack_in[u // 20], (t + 1) * STACK_LOADS)
                if u >= S_RING or since(t, 1):
                    pe.wait_ge(s_read, n - S_RING + 1)
                q_s, k_s, bank = stack["Q"][par], stack["K"][par], ps_s[u % S_RING]
                for h, tile, c, w, d in segments(u, False):
                    mm(bank[:, c:c + w], q_s[0:ROWS, h, tile * P:(tile + 1) * P], k_s[0:ROWS, h, 0:w],
                       start=True, stop=False)
                    last = mm(bank[:, d:d + P], ident_b[:], causal_s[:], start=False, stop=True)
                last.then_inc(s_full, 1)

            def scores_t(b, v, par):
                n = b * UNITS + v
                if v % 20 == 0:
                    pe.wait_ge(max_in[v // 20], (b + 1) * 48)
                    if not since(b, 1):
                        pe.wait_ge(ones_in, 2 * 16)
                if v >= T_RING or since(b, 1):
                    pe.wait_ge(p_ready, n - T_RING + 1)
                q_s, k_s, bank = stack["Q"][par], stack["K"][par], ps_t[v % T_RING]
                for h, tile, c, w, d in segments(v, True):
                    mm(bank[:, c:c + w], k_s[0:ROWS + PARTS, h, tile * P:(tile + 1) * P],
                       q_s[0:ROWS + PARTS, h, S - w:S], start=True, stop=False)
                    last = mm(bank[:, d:d + P], ident_b[:], causal_t[:], start=False, stop=True)
                last.then_inc(t_full, 1)

            def products(b, v, par):
                n = b * UNITS + v
                group = v // 10
                if v == 0:
                    pe.wait_ge(v_op_ready, 2 * (b + 1))
                if v % 10 == 0 and (group >= 2 or group == 0 and since(b, 1)):
                    pe.wait_ge(o_copied, b * 4 + group - 1)
                pe.wait_ge(p_ready, n + 1)
                for h, tile, c, w, _ in segments(v, True):
                    r = h % 4 * VC
                    last = mm(ps_o[group % 2][r:r + VC, S - w:S], v_op[par][:, tile, h, :], probs[:, v % P_RING, c:c + w],
                              start=(tile == 0), stop=(tile == NT - 1), skip_group_check=True)
                last.then_inc(pv_done, 1)

            def iteration(t, par, prep, cur, prev):
                last_job[:] = [None, None]
                for u in range(UNITS):
                    job = SIDE.get(u)
                    if job and present(job, prep, cur, prev):
                        side(t, job, par)
                    if cur:
                        scores(t, u, par)
                    if u >= T_LAG and cur:
                        scores_t(t, u - T_LAG, par)
                    elif u < T_LAG and prev:
                        scores_t(t - 1, u - T_LAG + UNITS, 1 - par)
                    if u >= PV_LAG and cur:
                        products(t, u - PV_LAG, par)
                    elif u < PV_LAG and prev:
                        products(t - 1, u - PV_LAG + UNITS, 1 - par)

            pe.wait_ge(const_ready, N_CONST)
            over_iterations(pe, iteration)


def kernel(**inputs):
    import numpy as np
    import concourse.bacc as bacc
    from concourse.bass_utils import run_bass_kernel_spmd

    nc = bacc.Bacc("TRN2", target_bir_lowering=False, num_devices=1)
    arrays = {
        "xT": np.ascontiguousarray(np.transpose(np.asarray(inputs["x"]), (0, 2, 1))),
        "ctxT": np.ascontiguousarray(np.transpose(np.asarray(inputs["ctx_1024"]), (0, 2, 1))),
        "x": np.ascontiguousarray(inputs["x"]),
        "wqT": np.ascontiguousarray(np.asarray(inputs["L0_xattn_Wq"]).T),
        "wkT": np.ascontiguousarray(np.asarray(inputs["L0_xattn_Wk"]).T),
        "wvT": np.ascontiguousarray(np.asarray(inputs["L0_xattn_Wv"]).T),
        "bq": np.ascontiguousarray(np.asarray(inputs["L0_xattn_bq"]).reshape(HALVES, P).T),
        "bk": np.ascontiguousarray(np.asarray(inputs["L0_xattn_bk"]).reshape(HALVES, P).T),
        "bv": np.ascontiguousarray(inputs["L0_xattn_bv"]),
        "gamma": np.ascontiguousarray(inputs["L0_xattn_gamma"]),
        "beta": np.ascontiguousarray(inputs["L0_xattn_beta"]),
    }
    aps = [nc.dram_tensor(f"in_{n}", a.shape, mybir.dt.from_np(a.dtype), kind="ExternalInput").ap()
           for n, a in arrays.items()]
    out = nc.dram_tensor("out", (B, S, D), F32, kind="ExternalOutput").ap()
    xattn(nc, *aps, out)
    r = run_bass_kernel_spmd(nc, [{f"in_{n}": a for n, a in arrays.items()}], core_ids=[0])
    return r.results[0]["out"]
```
